# Optimizing a Trainium2 kernel written in Bass

```python
import numpy as np
import jax
import jax.numpy as jnp

def _softmax(x, axis=-1):
    return jax.nn.softmax(x, axis=axis)

def _gelu(x):
    return jax.nn.gelu(x, approximate=True)

def _silu(x):
    return jax.nn.silu(x)

def _sigmoid(x):
    return jax.nn.sigmoid(x)

def _layernorm(x, axis=-1, eps=1e-05):
    m = jnp.mean(x, axis=axis, keepdims=True)
    v = jnp.var(x, axis=axis, keepdims=True)
    return (x - m) / jnp.sqrt(v + eps)

def _scatter_add(tgt, idx, src, axis=0):
    return tgt.at[idx].add(src)

def _segment_sum(src, seg, n):
    return jax.ops.segment_sum(src, seg, n)
kernel_name = 'mk_gnn_resnorm_d1_gnn_r8_e9716a'

def setup_inputs(seed: int=0):
    np.random.seed(seed)
    _w = jnp.asarray

    def _rec_inputs():
        import jax
        import jax.numpy as jnp
        _gk = jax.random.key(seed)
        x = -0.000202 + 1 * jax.random.normal(jax.random.fold_in(_gk, 1), (6250, 128), jnp.float32)
        src = jax.random.randint(jax.random.fold_in(_gk, 2), (100000,), 0, 6250, jnp.int32)
        dst = jax.random.randint(jax.random.fold_in(_gk, 3), (100000,), 0, 6250, jnp.int32)
        _o = jnp.argsort(dst, stable=True)
        src = src[_o]
        dst = dst[_o]
        return (x, src, dst)
    x, src, dst = _rec_inputs()

    def _L0_gnn_setup():
        import jax, jax.numpy as jnp
        import numpy as np
        N_NODES = 6250
        N_EDGES = 100000
        IN_FEATS = 128
        OUT_FEATS = 128
        key = jax.random.key(seed)
        k_feat, k_src, k_dst, k_w1, k_w2, k_lw = jax.random.split(key, 6)
        feat = jax.random.normal(k_feat, (N_NODES, IN_FEATS), dtype=jnp.float32)
        src_idx = jax.random.randint(k_src, (N_EDGES,), 0, N_NODES, dtype=jnp.int64 if jax.config.jax_enable_x64 else jnp.int32)
        dst_idx = jax.random.randint(k_dst, (N_EDGES,), 0, N_NODES, dtype=jnp.int64 if jax.config.jax_enable_x64 else jnp.int32)
        w1_lim = float(np.sqrt(6.0 / (2 * IN_FEATS + IN_FEATS)))
        w2_lim = float(np.sqrt(6.0 / (IN_FEATS + OUT_FEATS)))
        lw_lim = float(np.sqrt(2.0) * np.sqrt(6.0 / (IN_FEATS + OUT_FEATS)))
        weight1 = jax.random.uniform(k_w1, (2 * IN_FEATS, IN_FEATS), jnp.float32, -w1_lim, w1_lim)
        weight2 = jax.random.uniform(k_w2, (IN_FEATS, OUT_FEATS), jnp.float32, -w2_lim, w2_lim)
        loop_weight = jax.random.uniform(k_lw, (IN_FEATS, OUT_FEATS), jnp.float32, -lw_lim, lw_lim)
        bias = jnp.zeros((OUT_FEATS,), dtype=jnp.float32)
        return {'feat': feat, 'src_idx': src_idx, 'dst_idx': dst_idx, 'weight1': weight1, 'weight2': weight2, 'loop_weight': loop_weight, 'bias': bias}
    _L0_gnn_all = _L0_gnn_setup()
    _L0_gnn_in = {k: v for k, v in _L0_gnn_all.items() if k in ('weight1', 'weight2', 'loop_weight', 'bias')}
    del _L0_gnn_all
    return {'x': x, 'src': src, 'dst': dst, 'L0_gnn_weight1': _L0_gnn_in['weight1'], 'L0_gnn_weight2': _L0_gnn_in['weight2'], 'L0_gnn_loop_weight': _L0_gnn_in['loop_weight'], 'L0_gnn_bias': _L0_gnn_in['bias']}

def reference(x, src, dst, L0_gnn_weight1, L0_gnn_weight2, L0_gnn_loop_weight, L0_gnn_bias):
    import jax
    import jax.numpy as jnp

    def _L0_gnn_ref(feat, src_idx, dst_idx, weight1, weight2, loop_weight, bias):
        import jax, jax.numpy as jnp
        import numpy as np
        N_NODES = 6250
        N_EDGES = 100000
        IN_FEATS = 128
        OUT_FEATS = 128
        feat_msg = jnp.concatenate([feat[src_idx], feat[dst_idx]], axis=-1)
        e_msg = jnp.matmul(jax.nn.relu(jnp.matmul(feat_msg, weight1)), weight2)
        rst = jax.ops.segment_sum(e_msg, dst_idx, num_segments=feat.shape[0])
        rst = rst + bias + jnp.matmul(feat, loop_weight)
        return rst
    x = _layernorm(x + _L0_gnn_ref(x, src, dst, L0_gnn_weight1, L0_gnn_weight2, L0_gnn_loop_weight, L0_gnn_bias), axis=-1)
    return x

_drawn_inputs = setup_inputs


def setup_inputs(seed=0):
    import zlib

    import numpy as np

    out = dict(_drawn_inputs(seed))
    spreads = {'L0_gnn_bias': (0.0, 0.742)}
    factors = {}
    for name, (base, spread) in spreads.items():
        noise = np.random.default_rng([zlib.crc32(name.encode()), seed]).standard_normal(out[name].shape)
        drawn = base * np.exp(spread * noise) if base else spread * noise
        out[name] = jnp.asarray(drawn.astype(out[name].dtype))
    for name, factor in factors.items():
        out[name] = (out[name] * factor).astype(out[name].dtype)
    return out
```

```python
from contextlib import ExitStack

import concourse.bass as bass
from concourse import mybir

P = 128
CH = 8
HC = CH // 2

F32 = mybir.dt.float32
I32 = mybir.dt.int32
ALU = mybir.AluOpType
ACT = mybir.ActivationFunctionType
AX = mybir.AxisListType
EPS = 1e-5


def program(nc, x, src, dst, w1, w2, wl, bias, out, n_nodes):
    NG = src.shape[1] // CH - 2
    NI = NG // 2
    NT = out.shape[0] // P
    TB = 7
    NB = NT // TB
    assert NG % 2 == 0 and NT == NI and NT % TB == 0 and x.shape[0] >= n_nodes + P

    with ExitStack() as ctx:
        def sb(name, shape, dt=F32):
            return ctx.enter_context(nc.sbuf_tensor(name, shape, dt))

        def bank(name, shape):
            return ctx.enter_context(nc.psum_tensor(name, shape, F32))

        def sem(name):
            return ctx.enter_context(nc.semaphore(name))

        src_all = sb("src_all", [P, CH * (NG + 2)], I32)
        dst_all = sb("dst_all", [P, CH * NG], I32)
        dloc = sb("dloc", [P, CH * NG])
        src_now = sb("src_now", [P, 2, CH], I32)
        xg = sb("xg", [P, 2, CH, P])
        xgT = sb("xgT", [P, 2, HC, P])
        hot = sb("hot", [P, 2, CH, P])
        hotT = sb("hotT", [P, 2, HC, P])
        msg = sb("msg", [P, 2, HC, P])
        xwin = sb("xwin", [P, 2, P])
        xwinT = sb("xwinT", [P, P])
        bwin = sb("bwin", [P, 2, P])
        xt = sb("xt", [P, P])
        xtT = sb("xtT", [P, P])
        ST = sb("ST", [P, x.shape[0]])
        base = sb("base", [P, NT, P])
        w1a = sb("w1a", [P, P])
        w1b = sb("w1b", [P, P])
        w2s = sb("w2s", [P, P])
        wls = sb("wls", [P, P])
        bias_row = sb("bias_row", [1, P])
        ones = sb("ones", [P, P])
        ident = sb("ident", [P, P])
        iota = sb("iota", [P, P])
        before = sb("before", [P, P])
        ext = sb("ext", [P, 2, NG])
        col = sb("col", [P, 8])
        coli = sb("coli", [P, 2], I32)
        scaled = sb("scaled", [P, 3, NG + 1])
        table = sb("table", [1, NG + 1, 4], I32)
        stats = sb("stats", [P, TB, 6])
        mv = sb("mv", [P, TB, 2])
        rstd = sb("rstd", [P, TB])
        eps = sb("eps", [P, 1])
        Stile = sb("Stile", [P, TB, P])

        pxT = bank("pxT", [P, HC, P])
        phT = bank("phT", [P, HC, P])
        ppre = [bank(f"ppre{h}", [P, HC, P]) for h in range(2)]
        pS = bank("pS", [P, HC, P])
        pturn = bank("pturn", [P, HC, P])
        pprod = bank("pprod", [P, HC, P])
        piota = bank("piota", [P, HC, P])

        edges_in, weights_in, bias_in = sem("edges_in"), sem("weights_in"), sem("bias_in")
        consts_made, cleared, iota_in_psum = sem("consts_made"), sem("cleared"), sem("iota_in_psum")
        extremes, ext_turned, col_made, rows_made, table_made = (
            sem("extremes"), sem("ext_turned"), sem("col_made"), sem("rows_made"), sem("table_made"))
        src_staged, pool_turns, shifted = sem("src_staged"), sem("pool_turns"), sem("shifted")
        gathered = [[sem(f"gathered{b}{h}") for h in range(2)] for b in range(2)]
        win_in = [sem(f"win_in{b}") for b in range(2)]
        tile_in = sem("tile_in")
        x_turned, xT_copied = sem("x_turned"), sem("xT_copied")
        hot_made, hot_turned, hotT_copied = sem("hot_made"), sem("hot_turned"), sem("hotT_copied")
        turned, turn_copied = sem("turned"), sem("turn_copied")
        pre_made, relu_made, summed, added = sem("pre_made"), sem("relu_made"), sem("summed"), sem("added")
        prod_made, prod_kept = sem("prod_made"), sem("prod_kept")
        S_copied, y_made, y_kept, stats_made, mv_made, std_made, rstd_made, y_done, stored = (
            sem("S_copied"), sem("y_made"), sem("y_kept"), sem("stats_made"), sem("mv_made"),
            sem("std_made"), sem("rstd_made"), sem("y_done"), sem("stored"))

        def wait(eng, s, value):
            if not isinstance(value, int) or value > 0:
                eng.wait_ge(s, value)

        def turns(eng, step):
            step(0)
            with eng.Fori(1, NI) as i:
                step(i)

        def spilled(eng, step):
            with eng.If(eng.value_load(table[0:1, NG:NG + 1, 2:3], min_val=0, max_val=NG * NT) > 0):
                with eng.Fori(0, NG) as g:
                    n = eng.value_load(table[0:1, bass.ds(g, 1), 1:2], min_val=0, max_val=NT)
                    with eng.If(n > 0):
                        before_it = eng.value_load(table[0:1, bass.ds(g, 1), 2:3], min_val=0, max_val=NG * NT)
                        first = eng.value_load(table[0:1, bass.ds(g, 1), 0:1], min_val=0, max_val=n_nodes)
                        with eng.Fori(0, n) as k:
                            step(before_it + k, g, nc.s_assert_within(first + P * (k + 1), P, n_nodes))

        block = ctx.enter_context(nc.Block())

        @block.sync
        def _(sp):
            sp.dma_start(src_all[:, :], src).then_inc(edges_in, 16)
            sp.dma_start(dst_all[:, :], dst).then_inc(edges_in, 16)
            for tile, rows in ((w1a, w1[0:P, :]), (w1b, w1[P:2 * P, :]), (wls, wl), (w2s, w2)):
                sp.dma_start(tile[:, :], rows).then_inc(weights_in, 16)
            sp.dma_start(bias_row[:, :], bias.rearrange("(a n) -> a n", a=1)).then_inc(bias_in, 16)
            sp.wait_ge(table_made, 1)

            def step(i):
                for b in range(2):
                    g = 2 * i + b
                    start = sp.value_load(table[0:1, bass.ds(g, 1), 0:1] if not isinstance(i, int) else table[0:1, g:g + 1, 0:1],
                                          min_val=0, max_val=n_nodes)
                    wait(sp, turned, 3 * (i - 1) + (1 if b == 0 else 3))
                    sp.dma_start(xwin[:, b, :], x[bass.ds(start, P), :]).then_inc(win_in[b], 16)
                    if b == 0:
                        wait(sp, prod_kept, 3 * i - 1)
                        sp.dma_start(xt[:, :], x[bass.ds(P * i, P), :]).then_inc(tile_in, 16)
            turns(sp, step)

            def spilled_window(t, g, start):
                sp.wait_ge(turned, 3 * NI + t)
                sp.dma_start(xwin[:, 0, :], x[bass.ds(start, P), :]).then_inc(win_in[0], 16)
            spilled(sp, spilled_window)

            for k in range(NB):
                sp.wait_ge(y_done, TB * (k + 1))
                sp.dma_start(out[k * TB * P:(k + 1) * TB * P, :].rearrange("(t p) f -> p t f", p=P),
                             base[:, k * TB:(k + 1) * TB, :]).then_inc(stored, 16)
            sp.wait_ge(stored, 16 * NB)

        @block.gpsimd
        def _(pool):
            def gather(b, staged, used):
                wait(pool, src_staged, staged)
                wait(pool, x_turned, used)
                pool.sem_inc(pool_turns, 1)
                for j in range(CH):
                    pool.indirect_dma_start(
                        xg[:, b, j, :], None, x,
                        bass.IndirectOffsetOnAxis(ap=src_now[:, b, j:j + 1], axis=0),
                    ).then_inc(gathered[b][j // HC], 16)

            def step(i):
                for b in range(2):
                    gather(b, 2 * i + b + 1, 2 * (2 * i + b - 1))
            nc.gpsimd.iota(iota[:, :], [[1, P]], base=0, channel_multiplier=0,
                           allow_small_or_imprecise_dtypes=True).then_inc(consts_made, 1)
            nc.gpsimd.memset(ident[:, :], 0.0).then_inc(cleared, 1)
            nc.gpsimd.memset(before[:, :], 1.0).then_inc(cleared, 1)
            pool.wait_ge(cleared, 2)
            nc.gpsimd.affine_select(out=ident[:, :], in_=ident[:, :], compare_op=ALU.not_equal, fill=1.0,
                                    base=0, pattern=[[-1, P]], channel_multiplier=1).then_inc(consts_made, 1)
            nc.gpsimd.affine_select(out=before[:, :], in_=before[:, :], compare_op=ALU.is_gt, fill=0.0,
                                    base=0, pattern=[[1, P]], channel_multiplier=-1).then_inc(consts_made, 1)
            turns(pool, step)
            pool.wait_ge(table_made, 1)
            spilled(pool, lambda t, g, start: gather(0, NG + 2 + t + 1, 2 * (NG + t)))

        @block.scalar
        def _(act):
            def copy_xT(u, h):
                wait(act, x_turned, u + 1)
                wait(act, pre_made, u - 1)
                nc.scalar.copy(xgT[:, h], pxT[:, :, :]).then_inc(xT_copied, 1)

            def relu(u, h):
                wait(act, pre_made, u + 1)
                wait(act, summed, u - 1)
                nc.scalar.activation(msg[:, h], ppre[h][:, :, :], ACT.Relu).then_inc(relu_made, 1)

            def copy_turned(v, to, used):
                wait(act, turned, v + 1)
                wait(act, prod_made, used)
                nc.scalar.copy(to[:, :], pturn[:, 0, :]).then_inc(turn_copied, 1)

            def step(i):
                for b in range(2):
                    for h in range(2):
                        u = 4 * i + 2 * b + h
                        copy_xT(u, h)
                        if h == 0:
                            copy_turned(3 * i + 2 * b, xwinT, 3 * i if b == 0 else 3 * i + 1)
                        elif b == 0:
                            copy_turned(3 * i + 1, xtT, 3 * (i - 1) + 2)
                        if not (isinstance(i, int) and b == 0 and h == 0):
                            relu(u - 1, (h + 1) % 2)
            turns(act, step)
            relu(2 * NG - 1, 1)

            def spilled_window(t, g, start):
                u = 2 * (NG + t)
                copy_xT(u, 0)
                copy_turned(3 * NI + t, xwinT, 3 * NI + t)
                relu(u, 0)
                copy_xT(u + 1, 1)
                relu(u + 1, 1)
            act.wait_ge(table_made, 1)
            spilled(act, spilled_window)

            for k in range(NB):
                if k == 0:
                    act.wait_ge(added, NG + act.value_load(table[0:1, NG:NG + 1, 2:3], min_val=0, max_val=NG * NT))
                else:
                    act.wait_ge(y_made, TB * k)
                nc.scalar.copy(Stile[:, :, :], ST[:, k * TB * P:(k + 1) * TB * P].rearrange("f (t n) -> f t n", n=P)
                               ).then_inc(S_copied, 1)
                act.wait_ge(mv_made, k + 1)
                if k == 0:
                    act.wait_ge(consts_made, 3)
                nc.scalar.activation(rstd[:, :], mv[:, :, 1], ACT.Sqrt, bias=eps[:, 0:1]).then_inc(std_made, 1)

        @block.tensor
        def _(pe):
            def turn_x(u, b, h, filled):
                wait(pe, gathered[b][h], 16 * HC * filled)
                wait(pe, xT_copied, u)
                for j in range(HC):
                    last = nc.tensor.transpose(pxT[:, j, :], xg[:, b, h * HC + j, :], ident[:, :])
                last.then_inc(x_turned, 1)

            def turn_hot(u, b, h):
                wait(pe, hot_made, u + 1)
                wait(pe, hotT_copied, u)
                for j in range(HC):
                    last = nc.tensor.transpose(phT[:, j, :], hot[:, b, h * HC + j, :], ident[:, :])
                last.then_inc(hot_turned, 1)

            def turn_small(v, tile, arrived, count):
                wait(pe, arrived, count)
                wait(pe, turn_copied, v)
                nc.tensor.transpose(pturn[:, 0, :], tile, ident[:, :]).then_inc(turned, 1)

            def window(v):
                wait(pe, turn_copied, v + 1)
                wait(pe, prod_kept, v)
                nc.tensor.matmul(pprod[:, 0, :], xwinT[:, :], w1b[:, :], start=True, stop=True).then_inc(prod_made, 1)

            def node_tile(i):
                wait(pe, turn_copied, 3 * i + 2)
                wait(pe, prod_kept, 3 * i + 1)
                nc.tensor.matmul(pprod[:, 0, :], xtT[:, :], wls[:, :], start=True, stop=False)
                nc.tensor.matmul(pprod[:, 0, :], ones[0:1, :], bias_row[:, :], start=False, stop=True).then_inc(prod_made, 1)

            def pre(u, b, h, v):
                wait(pe, xT_copied, u + 1)
                wait(pe, hotT_copied, u + 1)
                wait(pe, relu_made, u - 1)
                if h == 0:
                    wait(pe, prod_kept, v + 1)
                for j in range(HC):
                    nc.tensor.matmul(ppre[h][:, j, :], xgT[:, h, j, :], w1a[:, :], start=True, stop=False)
                    last = nc.tensor.matmul(ppre[h][:, j, :], hotT[:, h, j, :], bwin[:, b, :], start=False, stop=True)
                last.then_inc(pre_made, 1)

            def sums(u, g, b, h):
                wait(pe, relu_made, u + 1)
                if h == 0:
                    wait(pe, added, g)
                for j in range(HC):
                    last = nc.tensor.matmul(pS[:, 0, :], msg[:, h, j, :], hot[:, b, h * HC + j, :],
                                            start=(h == 0 and j == 0), stop=(h == 1 and j == HC - 1))
                last.then_inc(summed, 1)

            pe.wait_ge(consts_made, 3)
            pe.wait_ge(extremes, 2)
            nc.tensor.transpose(phT[0:NG, 0, :], ext[:, 0, :], ident[:, :])
            nc.tensor.transpose(phT[0:NG, 1, :], ext[:, 1, :], ident[:, :]).then_inc(ext_turned, 1)
            pe.wait_ge(col_made, 7)
            nc.tensor.matmul(ppre[0][:, 0, 0:NG + 1], ones[0:NG, :], scaled[0:NG, 0, :], start=True, stop=True)
            nc.tensor.matmul(ppre[0][:, 1, 0:NG + 1], ones[0:NG, :], scaled[0:NG, 1, :], start=True, stop=True)
            nc.tensor.matmul(ppre[0][:, 2, 0:NG + 1], ones[0:NG, :], scaled[0:NG, 2, :], start=True, stop=True
                             ).then_inc(rows_made, 1)
            pe.wait_ge(weights_in, 64)
            pe.wait_ge(bias_in, 16)

            def step(i):
                for b in range(2):
                    g = 2 * i + b
                    for h in range(2):
                        u = 2 * g + h
                        turn_x(u, b, h, i + 1)
                        turn_hot(u, b, h)
                        if h == 0:
                            turn_small(3 * i + 2 * b, xwin[:, b, :], win_in[b], 16 * (i + 1))
                        elif b == 0:
                            turn_small(3 * i + 1, xt[:, :], tile_in, 16 * (i + 1))
                        first = isinstance(i, int) and b == 0
                        if h == 0:
                            if not first:
                                pre(u - 1, 1 - b, 1, None)
                            window(3 * i + 2 * b)
                            if not first:
                                sums(u - 2, g - 1, 1 - b, 0)
                        else:
                            pre(u - 1, b, 0, 3 * i + 2 * b)
                            if b == 0:
                                node_tile(i)
                            if not first:
                                sums(u - 2, g - 1, 1 - b, 1)
            turns(pe, step)
            pre(2 * NG - 1, 1, 1, None)
            sums(2 * NG - 2, NG - 1, 1, 0)
            sums(2 * NG - 1, NG - 1, 1, 1)

            def spilled_window(t, g, start):
                u = 2 * (NG + t)
                turn_x(u, 0, 0, NI + t + 1)
                turn_hot(u, 0, 0)
                turn_small(3 * NI + t, xwin[:, 0, :], win_in[0], 16 * (NI + t + 1))
                window(3 * NI + t)
                pre(u, 0, 0, 3 * NI + t)
                turn_x(u + 1, 0, 1, NI + t + 1)
                turn_hot(u + 1, 0, 1)
                pre(u + 1, 0, 1, None)
                sums(u, NG + t, 0, 0)
                sums(u + 1, NG + t, 0, 1)
            pe.wait_ge(table_made, 1)
            spilled(pe, spilled_window)

            for k in range(NB):
                pe.wait_ge(S_copied, k + 1)
                if k > 0:
                    pe.wait_ge(y_kept, 2 * k)
                for t in range(TB):
                    nc.tensor.matmul(ppre[t // HC][:, t % HC, :], Stile[:, t, :], w2s[:, :], start=True, stop=True
                                     ).then_inc(y_made, 1)

        @block.vector
        def _(dve):
            dve.wait_ge(edges_in, 32)
            for b in range(2):
                nc.vector.tensor_copy(src_now[:, b, :], src_all[:, b * CH:(b + 1) * CH]).then_inc(src_staged, 1)
            grouped = dst_all[:, :].rearrange("p (g j) -> p g j", j=CH)
            nc.vector.tensor_reduce(ext[:, 0, :], grouped, AX.X, ALU.min).then_inc(extremes, 1)
            nc.vector.tensor_reduce(ext[:, 1, :], grouped, AX.X, ALU.max).then_inc(extremes, 1)
            nc.vector.memset(ones[:, :], 1.0)
            nc.vector.memset(eps[:, :], EPS)
            dve.wait_ge(ext_turned, 1)
            nc.vector.tensor_reduce(col[0:NG, 0:1], phT[0:NG, 0, :], AX.X, ALU.min).then_inc(col_made, 1)
            nc.vector.tensor_reduce(col[0:NG, 1:2], phT[0:NG, 1, :], AX.X, ALU.max).then_inc(col_made, 1)
            dve.wait_ge(col_made, 2)
            nc.vector.tensor_tensor(coli[0:NG, 0:1], col[0:NG, 1:2], col[0:NG, 0:1], ALU.subtract).then_inc(col_made, 1)
            dve.wait_ge(col_made, 3)
            nc.vector.tensor_scalar(coli[0:NG, 1:2], coli[0:NG, 0:1], 7, None, ALU.arith_shift_right).then_inc(col_made, 1)
            dve.wait_ge(col_made, 4)
            dve.wait_ge(consts_made, 3)
            nc.vector.tensor_scalar(scaled[0:NG, 0, :], ident[0:NG, 0:NG + 1], col[0:NG, 0:1], None, ALU.mult).then_inc(col_made, 1)
            nc.vector.tensor_scalar(scaled[0:NG, 1, :], ident[0:NG, 0:NG + 1], coli[0:NG, 1:2], None, ALU.mult).then_inc(col_made, 1)
            nc.vector.tensor_scalar(scaled[0:NG, 2, :], before[0:NG, 0:NG + 1], coli[0:NG, 1:2], None, ALU.mult).then_inc(col_made, 1)
            nc.vector.tensor_copy(piota[:, 0, :], iota[:, :]).then_inc(iota_in_psum, 1)
            nc.vector.memset(ST[:, :], 0.0).then_inc(iota_in_psum, 1)
            dve.wait_ge(rows_made, 1)
            nc.vector.tensor_copy(table[0:1, :, 0:3], ppre[0][0:1, 0:3, 0:NG + 1].rearrange("p k g -> p g k")).then_inc(table_made, 1)
            nc.vector.tensor_tensor(dloc[:, :].rearrange("p (g j) -> p g j", j=CH), grouped,
                                    ppre[0][:, 0, 0:NG].unsqueeze(2).to_broadcast([P, NG, CH]), ALU.subtract
                                    ).then_inc(table_made, 1)
            dve.wait_ge(table_made, 2)
            dve.wait_ge(iota_in_psum, 2)

            def make_hot(g, b, h, used):
                c = CH * g + h * HC
                wait(dve, summed, used)
                d = dloc[:, bass.ds(c, HC)]
                nc.vector.tensor_tensor(hot[:, b, h * HC:(h + 1) * HC, :],
                                        piota[:, 0:1, :].to_broadcast([P, HC, P]),
                                        d.unsqueeze(2).to_broadcast([P, HC, P]), ALU.is_equal).then_inc(hot_made, 1)

            def copy_hotT(u, h):
                wait(dve, hot_turned, u + 1)
                wait(dve, pre_made, u - 1)
                nc.vector.tensor_copy(hotT[:, h], phT[:, :, :]).then_inc(hotT_copied, 1)

            def copy_bwin(b, v, used):
                wait(dve, prod_made, v + 1)
                wait(dve, pre_made, used)
                nc.vector.tensor_copy(bwin[:, b, :], pprod[:, 0, :]).then_inc(prod_kept, 1)

            def add_sums(g, start):
                wait(dve, summed, 2 * g + 2)
                wait(dve, added, g)
                part = ST[:, bass.ds(start, P)]
                nc.vector.tensor_tensor(part, pS[:, 0, :], part, ALU.add).then_inc(added, 1)

            def window_start(g):
                return dve.value_load(table[0:1, bass.ds(g, 1), 0:1], min_val=0, max_val=n_nodes)

            def step(i):
                for b in range(2):
                    g = 2 * i + b
                    for h in range(2):
                        u = 2 * g + h
                        make_hot(g, b, h, u - 3)
                        copy_hotT(u, h)
                        if h == 0:
                            if not isinstance(i, int):
                                add_sums(g - 2, window_start(g - 2))
                            copy_bwin(b, 3 * i + 2 * b, 2 * (g - 1))
                        else:
                            wait(dve, x_turned, u + 1)
                            nc.vector.tensor_copy(src_now[:, b, :], src_all[:, bass.ds(CH * (g + 2), CH)]
                                                  ).then_inc(src_staged, 1)
                            if b == 0:
                                wait(dve, prod_made, 3 * i + 2)
                                nc.vector.tensor_tensor(base[:, bass.ds(i, 1), :], pprod[:, 0:1, :],
                                                        xt[:, :].unsqueeze(1), ALU.add).then_inc(prod_kept, 1)
            turns(dve, step)
            for b in range(2):
                add_sums(NG - 2 + b, window_start(NG - 2 + b))

            def spilled_window(t, g, start):
                u = 2 * (NG + t)
                nc.vector.tensor_copy(src_now[:, 0, :], src_all[:, bass.ds(CH * g, CH)]).then_inc(src_staged, 1)
                d = dloc[:, bass.ds(CH * g, CH)]
                nc.vector.tensor_scalar(d, d, float(-P), None, ALU.add).then_inc(shifted, 1)
                dve.wait_ge(shifted, t + 1)
                make_hot(g, 0, 0, u)
                make_hot(g, 0, 1, u)
                copy_hotT(u, 0)
                copy_bwin(0, 3 * NI + t, u)
                copy_hotT(u + 1, 1)
                add_sums(NG + t, start)
            spilled(dve, spilled_window)

            for k in range(NB):
                for n in range(2):
                    a, z = (0, HC) if n == 0 else (HC, TB)
                    dve.wait_ge(y_made, TB * k + z)
                    rows = base[:, k * TB + a:k * TB + z, :]
                    nc.vector.tensor_tensor(rows, ppre[n][:, 0:z - a, :], rows, ALU.add).then_inc(y_kept, 1)
                dve.wait_ge(y_kept, 2 * k + 2)
                for t in range(TB):
                    nc.vector.bn_stats(stats[:, t, :], base[:, k * TB + t, :]).then_inc(stats_made, 1)
                for t in range(TB):
                    dve.wait_ge(stats_made, TB * k + t + 1)
                    last = nc.vector.bn_aggr(mv[:, t, :], stats[:, t, :])
                last.then_inc(mv_made, 1)
                dve.wait_ge(std_made, k + 1)
                nc.vector.reciprocal(rstd[:, :], rstd[:, :]).then_inc(rstd_made, 1)
                dve.wait_ge(rstd_made, k + 1)
                for t in range(TB):
                    rows = base[:, k * TB + t, :]
                    nc.vector.tensor_scalar(rows, rows, mv[:, t, 0:1], rstd[:, t:t + 1], ALU.subtract, ALU.mult
                                            ).then_inc(y_done, 1)


def kernel(x, src, dst, L0_gnn_weight1, L0_gnn_weight2, L0_gnn_loop_weight, L0_gnn_bias):
    import numpy as np
    import concourse.bacc as bacc
    from concourse.bass_utils import run_bass_kernel_spmd as run

    x, src, dst = np.asarray(x), np.asarray(src), np.asarray(dst)
    n_nodes, n_edges = x.shape[0], src.shape[0]
    tiles = -(-n_nodes // P)
    groups = 2 * tiles
    assert groups * CH * P >= n_edges

    def edge_table(a, fill, n):
        a = np.concatenate([a, np.full(n * CH * P - a.shape[0], fill, a.dtype)])
        return np.ascontiguousarray(a.reshape(n * CH, P).T)

    arrays = {
        "x": np.concatenate([x, np.zeros(((tiles + 1) * P - n_nodes, x.shape[1]), x.dtype)]),
        "src": edge_table(src, 0, groups + 2),
        "dst": edge_table(dst, n_nodes, groups),
        "w1": np.asarray(L0_gnn_weight1), "w2": np.asarray(L0_gnn_weight2),
        "wl": np.asarray(L0_gnn_loop_weight), "bias": np.asarray(L0_gnn_bias),
    }
    nc = bacc.Bacc("TRN2", target_bir_lowering=False, num_devices=1)
    aps = [nc.dram_tensor(name, a.shape, mybir.dt.from_np(a.dtype), kind="ExternalInput").ap()
           for name, a in arrays.items()]
    out = nc.dram_tensor("out", (tiles * P, x.shape[1]), F32, kind="ExternalOutput").ap()
    program(nc, *aps, out, n_nodes)
    r = run(nc, [arrays], core_ids=[0])
    return r.results[0]["out"][:n_nodes]
```

```python
from contextlib import ExitStack

import concourse.bass as bass
from concourse import mybir

P = 128
CH = 8
HC = CH // 2
LAG = 2

F32 = mybir.dt.float32
BF16 = mybir.dt.bfloat16
I32 = mybir.dt.int32
ALU = mybir.AluOpType
ACT = mybir.ActivationFunctionType
AX = mybir.AxisListType
EPS = 1e-5


def program(nc, x, src, dst, w1, w2, wl, bias, out, n_nodes, n_chunks):
    NG = dst.shape[1] // CH
    NI = NG // 2
    NT = out.shape[0] // P
    assert NG % 2 == 0 and NT == NI and NT > LAG and x.shape[0] >= NT * P + P and NG + 1 <= P

    with ExitStack() as ctx:
        def sb(name, shape, dt=F32):
            return ctx.enter_context(nc.sbuf_tensor(name, shape, dt))

        def bank(name):
            return ctx.enter_context(nc.psum_tensor(name, [P, HC, P], F32))

        def sem(name):
            return ctx.enter_context(nc.semaphore(name))

        src_all = sb("src_all", [P, CH * (NG + 2)], I32)
        dst_all = sb("dst_all", [P, CH * NG], I32)
        dloc = sb("dloc", [P, CH * (NG + 1)])
        src_now = sb("src_now", [P, 2, CH], I32)
        xg = sb("xg", [P, 2, CH, P])
        xgT = sb("xgT", [P, 2, HC, P])
        hot = sb("hot", [P, 2, CH, P])
        hotT = sb("hotT", [P, 2, HC, P], BF16)
        msg = sb("msg", [P, 2, HC, P])
        xwin = sb("xwin", [P, 2, P])
        xwinT = sb("xwinT", [P, P])
        bwin = sb("bwin", [P, 2, 3, P], BF16)
        brest = sb("brest", [P, P])
        xt = sb("xt", [P, P])
        xtT = sb("xtT", [P, P])
        ST = sb("ST", [P, x.shape[0]])
        ST_now = sb("ST_now", [P, LAG, P])
        base = sb("base", [P, NT, P])
        y = sb("y", [P, LAG, P])
        y_out = sb("y_out", [P, LAG, P])
        stats = sb("stats", [P, LAG, 6])
        mv = sb("mv", [P, LAG, 2])
        std = sb("std", [P, LAG])
        rstd = sb("rstd", [P, LAG])
        w1s = sb("w1s", [P, 2, P])
        w2s = sb("w2s", [P, P])
        wls = sb("wls", [P, P])
        bias_row = sb("bias_row", [1, P])
        ones = sb("ones", [P, P])
        eps = sb("eps", [P, 1])
        ident = sb("ident", [P, P])
        iota = sb("iota", [P, P])
        before = sb("before", [P, P])
        lane = sb("lane", [P, 1], I32)
        ext = sb("ext", [P, 2, NG])
        col = sb("col", [P, 3])
        coli = sb("coli", [P, 3], I32)
        scaled = sb("scaled", [P, 4, NG + 1])
        START, SPILLED, SPILLED_BEFORE, LATE_BEFORE = range(4)
        table = sb("table", [1, NG + 1, 4], I32)

        pxT, phT, ppre = bank("pxT"), bank("phT"), [bank("ppre0"), bank("ppre1")]
        pS = bank("pS")
        pturn = bank("pturn")
        pprod = bank("pprod")
        piota = bank("piota")

        src_head_in, src_in, dst_in, w1_in, weights_in = (
            sem("src_head_in"), sem("src_in"), sem("dst_in"), sem("w1_in"), sem("weights_in"))
        cleared, consts_made, vec_consts_made, ST_cleared, iota_in_psum = (
            sem("cleared"), sem("consts_made"), sem("vec_consts_made"), sem("ST_cleared"), sem("iota_in_psum"))
        extremes, ext_turned, col_made, scaled_made, rows_made, table_made = (
            sem("extremes"), sem("ext_turned"), sem("col_made"), sem("scaled_made"), sem("rows_made"),
            sem("table_made"))
        src_staged, pool_turns, shifted = sem("src_staged"), sem("pool_turns"), sem("shifted")
        gathered = [[sem(f"gathered{b}{h}") for h in range(2)] for b in range(2)]
        win_in = [sem(f"win_in{b}") for b in range(2)]
        tile_in = sem("tile_in")
        x_turned, xT_copied = sem("x_turned"), sem("xT_copied")
        hot_made, hot_turned, hotT_copied = sem("hot_made"), sem("hot_turned"), sem("hotT_copied")
        turned, turn_copied = sem("turned"), sem("turn_copied")
        prod_made, prod_kept = sem("prod_made"), sem("prod_kept")
        bwin_parts, bwin_made = sem("bwin_parts"), sem("bwin_made")
        pre_made, relu_made, summed, added = sem("pre_made"), sem("relu_made"), sem("summed"), sem("added")
        ST_taken, stats_made, mv_made, root_made, rstd_made, y_normed, stored = (
            sem("ST_taken"), sem("stats_made"), sem("mv_made"), sem("root_made"), sem("rstd_made"),
            sem("y_normed"), sem("stored"))
        aggr_turns = sem("aggr_turns")

        def wait(eng, s, value):
            if not isinstance(value, int) or value > 0:
                eng.wait_ge(s, value)

        def turns(eng, step):
            for i in range(LAG + 1):
                step(i)
            eng.wait_ge(table_made, 1)
            windows = look_up(eng, NG, SPILLED_BEFORE, NG * NT)
            late = look_up(eng, NG, LATE_BEFORE, NG)
            with eng.Fori(LAG + 1, NI) as i:
                step(i)
            return windows, late

        def behind(i, turn):
            return not isinstance(i, int) or i > turn

        def product(i, n):
            return (3 * i if isinstance(i, int) else 4 * i - LAG) + n

        PRODUCTS = 4 * NI - LAG

        def look_up(eng, g, what, top):
            return eng.value_load(table[0:1, bass.ds(g, 1), what:what + 1], min_val=0, max_val=top)

        def spilled(eng, windows, step):
            with eng.If(windows > 0):
                with eng.Fori(0, NG) as g:
                    n = look_up(eng, g, SPILLED, NT)
                    with eng.If(n > 0):
                        t0 = look_up(eng, g, SPILLED_BEFORE, NG * NT)
                        first = look_up(eng, g, START, n_nodes)
                        with eng.Fori(0, n) as k:
                            step(t0 + k, g, nc.s_assert_within(first + P * (k + 1), P, n_nodes))

        NORMS = NT - LAG + 1

        def redone(eng, windows, late, step):
            with eng.If(windows + late > 0):
                with eng.Fori(0, NT) as tile:
                    step(tile, NORMS + tile, PRODUCTS + 1 + windows + tile)

        block = ctx.enter_context(nc.Block())

        @block.sync
        def _(sp):
            head = 2 * CH
            sp.dma_start(src_all[:, 0:head], src[:, 0:head]).then_inc(src_head_in, 16)
            sp.dma_start(dst_all[:, :], dst).then_inc(dst_in, 16)
            sp.dma_start(src_all[:, head:], src[:, head:]).then_inc(src_in, 16)
            sp.wait_ge(table_made, 1)

            def load_window(b, start, turned_before):
                wait(sp, turned, turned_before)
                sp.dma_start(xwin[:, b, :], x[bass.ds(start, P), :]).then_inc(win_in[b], 16)

            def store(tile, k, n=1):
                sp.wait_ge(y_normed, k + 1)
                sp.dma_start(out[bass.ds(P * tile, P * n), :].rearrange("(t p) f -> p t f", p=P), y_out[:, 0:n, :]
                             ).then_inc(stored, 16)

            def step(i):
                load_window(0, look_up(sp, 2 * i, START, n_nodes), 3 * (i - 1) + 1)
                if behind(i, 0):
                    wait(sp, prod_kept, product(i - 1, 1) + 1)
                sp.dma_start(xt[:, :], x[bass.ds(P * i, P), :]).then_inc(tile_in, 16)
                load_window(1, look_up(sp, 2 * i + 1, START, n_nodes), 3 * (i - 1) + 3)
                if behind(i, LAG):
                    store(i - LAG - 1, i - LAG - 1)
            windows, late = turns(sp, step)
            store(NI - LAG - 1, NI - LAG - 1)
            spilled(sp, windows, lambda t, g, start: load_window(0, start, 3 * NI + t))
            store(NT - LAG, NORMS - 1, LAG)
            redone(sp, windows, late, lambda tile, k, v: store(tile, k))
            sp.wait_ge(stored, 16 * NORMS)
            with sp.If(windows + late > 0):
                sp.wait_ge(stored, 16 * (NORMS + NT))

        @block.gpsimd
        def _(pool):
            def gather(b, indices, x_turned_before, real=CH):
                wait(pool, x_turned, x_turned_before)
                pool.sem_inc(pool_turns, 1)
                for j in range(real):
                    count = 1 if j < real - 1 else CH - real + 1
                    pool.indirect_dma_start(
                        xg[:, b, j, :], None, x,
                        bass.IndirectOffsetOnAxis(ap=indices[:, j:j + 1], axis=0),
                    ).then_inc(gathered[b][j // HC], 16 * count)

            nc.gpsimd.memset(ident[:, :], 0.0).then_inc(cleared, 1)
            nc.gpsimd.memset(before[:, :], 1.0).then_inc(cleared, 1)
            nc.gpsimd.iota(iota[:, :], [[1, P]], base=0, channel_multiplier=0,
                           allow_small_or_imprecise_dtypes=True).then_inc(consts_made, 1)
            nc.gpsimd.iota(lane[:, :], [[0, 1]], base=0, channel_multiplier=1).then_inc(consts_made, 1)
            pool.wait_ge(cleared, 2)
            nc.gpsimd.affine_select(out=ident[:, :], in_=ident[:, :], compare_op=ALU.not_equal, fill=1.0,
                                    base=0, pattern=[[-1, P]], channel_multiplier=1).then_inc(consts_made, 1)
            nc.gpsimd.affine_select(out=before[:, :], in_=before[:, :], compare_op=ALU.is_gt, fill=0.0,
                                    base=0, pattern=[[1, P]], channel_multiplier=-1).then_inc(consts_made, 1)

            pool.wait_ge(src_head_in, 16)
            for b in range(2):
                gather(b, src_all[:, b * CH:(b + 1) * CH], 0)
            with pool.Fori(1, NI - 1) as i:
                for b in range(2):
                    pool.wait_ge(src_staged, 2 * i + b - 1)
                    gather(b, src_now[:, b, :], 2 * (2 * i + b - 1))
            for b in range(2):
                pool.wait_ge(src_staged, NG - 3 + b)
                gather(b, src_now[:, b, :], 2 * (NG - 3 + b), min(CH, n_chunks - CH * (NG - 2 + b)))

            pool.wait_ge(table_made, 1)
            windows = look_up(pool, NG, SPILLED_BEFORE, NG * NT)

            def spilled_window(t, g, start):
                pool.wait_ge(src_staged, NG + t + 1)
                gather(0, src_now[:, 0, :], 2 * (NG + t))
            spilled(pool, windows, spilled_window)

        @block.scalar
        def _(act):
            act.dma_start(w1s[:, :, :], w1.rearrange("(k p) f -> p k f", k=2)).then_inc(w1_in, 16)
            act.dma_start(wls[:, :], wl).then_inc(weights_in, 16)
            act.dma_start(bias_row[:, :], bias.rearrange("(a n) -> a n", a=1)).then_inc(weights_in, 16)
            act.dma_start(w2s[:, :], w2).then_inc(weights_in, 16)
            nc.scalar.preload_act_table(ACT.Sqrt)
            nc.scalar.memzero(ST[:, :]).then_inc(ST_cleared, 1)

            def copy_xT(u, h):
                wait(act, x_turned, u + 1)
                wait(act, pre_made, u - 1)
                nc.scalar.copy(xgT[:, h], pxT[:, :, :]).then_inc(xT_copied, 1)

            def relu(u, h):
                wait(act, pre_made, u + 1)
                wait(act, summed, u - 1)
                nc.scalar.activation(msg[:, h], ppre[h][:, :, :], ACT.Relu).then_inc(relu_made, 1)

            def copy_turned(v, to, products_before):
                wait(act, turned, v + 1)
                wait(act, prod_made, products_before)
                nc.scalar.copy(to[:, :], pturn[:, 0, :]).then_inc(turn_copied, 1)

            def root(k, n=1):
                wait(act, mv_made, k + 1)
                wait(act, y_normed, k)
                nc.scalar.activation(std[:, 0:n], mv[:, 0:n, 1], ACT.Sqrt, bias=eps[:, 0:1]).then_inc(root_made, 1)

            def step(i):
                for b in range(2):
                    for h in range(2):
                        u = 4 * i + 2 * b + h
                        copy_xT(u, h)
                        if (b, h) == (0, 0):
                            copy_turned(3 * i, xwinT, product(i - 1, 2) + 1 if behind(i, 0) else 0)
                        elif (b, h) == (0, 1):
                            copy_turned(3 * i + 1, xtT, product(i - 1, 1) + 1 if behind(i, 0) else 0)
                        elif (b, h) == (1, 0):
                            copy_turned(3 * i + 2, xwinT, product(i, 0) + 1)
                        if behind(u, 0):
                            relu(u - 1, (h + 1) % 2)
                        if (b, h) == (0, 0) and behind(i, LAG):
                            root(i - LAG - 1)
            act.wait_ge(vec_consts_made, 3)
            windows, late = turns(act, step)
            root(NI - LAG - 1)
            relu(2 * NG - 1, 1)

            def spilled_window(t, g, start):
                u = 2 * (NG + t)
                copy_xT(u, 0)
                copy_turned(3 * NI + t, xwinT, PRODUCTS + t)
                relu(u, 0)
                copy_xT(u + 1, 1)
                relu(u + 1, 1)
            spilled(act, windows, spilled_window)
            root(NORMS - 1, LAG)
            redone(act, windows, late, lambda tile, k, v: root(k))

        @block.tensor
        def _(pe):
            def turn_x(u, b, h, fills):
                pe.wait_ge(gathered[b][h], 16 * HC * fills)
                wait(pe, xT_copied, u)
                for j in range(HC):
                    last = nc.tensor.transpose(pxT[:, j, :], xg[:, b, h * HC + j, :], ident[:, :])
                last.then_inc(x_turned, 1)

            def turn_hot(u, b, h, made):
                wait(pe, hot_made, made)
                wait(pe, hotT_copied, u)
                for j in range(HC):
                    last = nc.tensor.transpose(phT[:, j, :], hot[:, b, h * HC + j, :], ident[:, :])
                last.then_inc(hot_turned, 1)

            def turn_small(v, tile, arrived, fills):
                wait(pe, arrived, 16 * fills)
                wait(pe, turn_copied, v)
                nc.tensor.transpose(pturn[:, 0, :], tile, ident[:, :]).then_inc(turned, 1)

            def window_product(n_turned, v):
                wait(pe, turn_copied, n_turned)
                wait(pe, prod_kept, v)
                nc.tensor.matmul(pprod[:, 0, :], xwinT[:, :], w1s[:, 1, :], start=True, stop=True).then_inc(prod_made, 1)

            def tile_product(n_turned, v):
                wait(pe, turn_copied, n_turned)
                wait(pe, prod_kept, v)
                nc.tensor.matmul(pprod[:, 0, :], xtT[:, :], wls[:, :], start=True, stop=False)
                nc.tensor.matmul(pprod[:, 0, :], ones[0:1, :], bias_row[:, :], start=False, stop=True
                                 ).then_inc(prod_made, 1)

            def sum_product(k, v, n=1):
                wait(pe, ST_taken, k + 1)
                wait(pe, prod_kept, v)
                for t in range(n):
                    last = nc.tensor.matmul(pprod[:, t, :], ST_now[:, t, :], w2s[:, :], start=True, stop=True)
                last.then_inc(prod_made, 1)

            def pre(u, b, h, bwins, chunks=HC):
                wait(pe, xT_copied, u + 1)
                wait(pe, hotT_copied, u + 1)
                wait(pe, relu_made, u - 1)
                if h == 0:
                    wait(pe, bwin_made, bwins)
                for j in range(chunks):
                    nc.tensor.matmul(ppre[h][:, j, :], xgT[:, h, j, :], w1s[:, 0, :], start=True, stop=False)
                    for part in range(3):
                        last = nc.tensor.matmul(ppre[h][:, j, :], hotT[:, h, j, :], bwin[:, b, part, :],
                                                start=False, stop=(part == 2))
                last.then_inc(pre_made, 1)

            def sums(u, groups_before, b, h, chunks=HC):
                wait(pe, relu_made, u + 1)
                if h == 0:
                    wait(pe, added, groups_before)
                for j in range(chunks):
                    last = nc.tensor.matmul(pS[:, 0, :], msg[:, h, j, :], hot[:, b, h * HC + j, :],
                                            start=(h == 0 and j == 0), stop=(h == 1 and j == chunks - 1))
                last.then_inc(summed, 1)

            pe.wait_ge(consts_made, 4)
            pe.wait_ge(vec_consts_made, 3)
            pe.wait_ge(extremes, 2)
            for k in range(2):
                last = nc.tensor.transpose(phT[0:NG, k, :], ext[:, k, :], ident[:, :])
            last.then_inc(ext_turned, 1)
            turn_x(0, 0, 0, 1)
            pe.wait_ge(scaled_made, 4)
            for k in range(4):
                last = nc.tensor.matmul(ppre[0][:, k, 0:NG + 1], ones[0:NG, :], scaled[0:NG, k, :],
                                        start=True, stop=True)
            last.then_inc(rows_made, 1)
            pe.wait_ge(w1_in, 16)
            pe.wait_ge(weights_in, 48)

            def step(i):
                for b in range(2):
                    g = 2 * i + b
                    for h in range(2):
                        u = 2 * g + h
                        if behind(u, 0):
                            turn_x(u, b, h, i + 1)
                        turn_hot(u, b, h, u + 1)
                        if h == 0:
                            turn_small(3 * i + 2 * b, xwin[:, b, :], win_in[b], i + 1)
                        elif b == 0:
                            turn_small(3 * i + 1, xt[:, :], tile_in, i + 1)
                        if h == 0:
                            if behind(u, 0):
                                pre(u - 1, 1 - b, 1, None)
                            window_product(3 * i + 2 * b + 1, product(i, 2 * b))
                            if behind(u, 1):
                                sums(u - 2, g - 1, 1 - b, 0)
                        else:
                            pre(u - 1, b, 0, g + 1)
                            if b == 0:
                                tile_product(3 * i + 2, product(i, 1))
                            elif behind(i, LAG - 1):
                                sum_product(i - LAG, product(i, 3))
                            if behind(u, 1):
                                sums(u - 2, g - 1, 1 - b, 1)
            windows, late = turns(pe, step)
            chunks = n_chunks - 2 * HC * NG + HC
            pre(2 * NG - 1, 1, 1, None, chunks)
            sums(2 * NG - 2, NG - 1, 1, 0)
            sums(2 * NG - 1, NG - 1, 1, 1, chunks)

            def spilled_window(t, g, start):
                u = 2 * (NG + t)
                turn_x(u, 0, 0, NI + t + 1)
                turn_hot(u, 0, 0, u + 2)
                turn_small(3 * NI + t, xwin[:, 0, :], win_in[0], NI + t + 1)
                window_product(3 * NI + t + 1, PRODUCTS + t)
                pre(u, 0, 0, NG + t + 1)
                turn_x(u + 1, 0, 1, NI + t + 1)
                turn_hot(u + 1, 0, 1, u + 3)
                pre(u + 1, 0, 1, None)
                sums(u, NG + t, 0, 0)
                sums(u + 1, NG + t, 0, 1)
            spilled(pe, windows, spilled_window)
            sum_product(NORMS - 1, PRODUCTS + windows, LAG)
            redone(pe, windows, late, lambda tile, k, v: sum_product(k, v))

        @block.vector
        def _(dve):
            nc.vector.memset(ones[:, :], 1.0).then_inc(vec_consts_made, 1)
            nc.vector.memset(eps[:, :], EPS).then_inc(vec_consts_made, 1)
            nc.vector.memset(dloc[:, CH * NG:], -1.0).then_inc(vec_consts_made, 1)
            dve.wait_ge(consts_made, 4)
            nc.vector.tensor_copy(piota[:, 0, :], iota[:, :]).then_inc(iota_in_psum, 1)
            nc.vector.tensor_scalar(coli[:, 2:3], lane[:, :], 1, 7, ALU.arith_shift_right, ALU.logical_shift_left
                                    ).then_inc(col_made, 1)
            dve.wait_ge(dst_in, 16)
            grouped = dst_all[:, :].rearrange("p (g j) -> p g j", j=CH)
            for k, op in enumerate((ALU.min, ALU.max)):
                nc.vector.tensor_reduce(ext[:, k, :], grouped, AX.X, op).then_inc(extremes, 1)
            dve.wait_ge(ext_turned, 1)
            for k, op in enumerate((ALU.min, ALU.max)):
                nc.vector.tensor_reduce(col[0:NG, k:k + 1], phT[0:NG, k, :], AX.X, op).then_inc(col_made, 1)
            dve.wait_ge(col_made, 3)
            least, greatest, late = (col[0:NG, k:k + 1] for k in range(3))
            nc.vector.tensor_tensor(coli[0:NG, 0:1], greatest, least, ALU.subtract).then_inc(col_made, 1)
            nc.vector.scalar_tensor_tensor(late, coli[0:NG, 2:3], float(-P * (LAG - 1)), least, ALU.add, ALU.is_gt
                                           ).then_inc(col_made, 1)
            dve.wait_ge(col_made, 5)
            nc.vector.tensor_scalar(coli[0:NG, 1:2], coli[0:NG, 0:1], 7, None, ALU.arith_shift_right
                                    ).then_inc(col_made, 1)
            dve.wait_ge(col_made, 6)
            windows = coli[0:NG, 1:2]
            for k, (weight, value) in enumerate(((ident, least), (ident, windows), (before, windows), (before, late))):
                nc.vector.tensor_scalar(scaled[0:NG, k, :], weight[0:NG, 0:NG + 1], value, None, ALU.mult
                                        ).then_inc(scaled_made, 1)
            dve.wait_ge(rows_made, 1)
            nc.vector.tensor_copy(table[0:1, :, :], ppre[0][0:1, :, 0:NG + 1].rearrange("p k g -> p g k")
                                  ).then_inc(table_made, 1)
            nc.vector.tensor_tensor(dloc[:, 0:CH * NG].rearrange("p (g j) -> p g j", j=CH), grouped,
                                    ppre[0][:, START, 0:NG].unsqueeze(2).to_broadcast([P, NG, CH]), ALU.subtract
                                    ).then_inc(table_made, 1)
            dve.wait_ge(table_made, 2)
            dve.wait_ge(iota_in_psum, 1)
            dve.wait_ge(vec_consts_made, 3)

            def make_hot(g, b, h, halves_before):
                wait(dve, summed, halves_before)
                d = dloc[:, bass.ds(CH * g + h * HC, HC)]
                nc.vector.tensor_tensor(hot[:, b, h * HC:(h + 1) * HC, :],
                                        piota[:, 0:1, :].to_broadcast([P, HC, P]),
                                        d.unsqueeze(2).to_broadcast([P, HC, P]), ALU.is_equal).then_inc(hot_made, 1)

            def copy_hotT(u, h):
                wait(dve, hot_turned, u + 1)
                wait(dve, pre_made, u - 1)
                nc.vector.tensor_copy(hotT[:, h], phT[:, :, :]).then_inc(hotT_copied, 1)

            def keep_window(b, g, v, halves_before):
                wait(dve, prod_made, v + 1)
                wait(dve, pre_made, halves_before)
                parts = [bwin[:, b, n, :] for n in range(3)]
                nc.vector.tensor_copy(parts[0], pprod[:, 0, :]).then_inc(bwin_parts, 1)
                dve.wait_ge(bwin_parts, 3 * g + 1)
                nc.vector.tensor_tensor(brest[:, :], pprod[:, 0, :], parts[0], ALU.subtract).then_inc(prod_kept, 1)
                dve.wait_ge(prod_kept, v + 1)
                nc.vector.tensor_copy(parts[1], brest[:, :]).then_inc(bwin_parts, 1)
                dve.wait_ge(bwin_parts, 3 * g + 2)
                nc.vector.tensor_tensor(parts[2], brest[:, :], parts[1], ALU.subtract).then_inc(bwin_parts, 1)
                dve.wait_ge(bwin_parts, 3 * g + 3)
                dve.sem_inc(bwin_made, 1)

            def add_sums(g, start):
                wait(dve, summed, 2 * g + 2)
                wait(dve, added, g)
                part = ST[:, bass.ds(start, P)]
                nc.vector.tensor_tensor(part, pS[:, 0, :], part, ALU.add).then_inc(added, 1)

            def take_sums(tile, k, groups, v, n=1):
                wait(dve, added, groups)
                wait(dve, prod_made, v)
                nc.vector.tensor_copy(ST_now[:, 0:n, :].rearrange("f t n -> f (t n)"),
                                      ST[:, bass.ds(P * tile, P * n)]).then_inc(ST_taken, 1)

            def keep_tile(tile, k, v, n=1):
                wait(dve, prod_made, v + 1)
                nc.vector.tensor_tensor(y[:, 0:n, :], pprod[:, 0:n, :], base[:, bass.ds(tile, n), :], ALU.add
                                        ).then_inc(prod_kept, 1)
                dve.wait_ge(prod_kept, v + 1)
                for t in range(n):
                    last = nc.vector.bn_stats(stats[:, t, :], y[:, t, :])
                last.then_inc(stats_made, 1)
                dve.wait_ge(stats_made, k + 1)
                dve.sem_inc(aggr_turns, 1)
                for t in range(n):
                    last = nc.vector.bn_aggr(mv[:, t, :], stats[:, t, :])
                last.then_inc(mv_made, 1)

            def normalise(k, n=1):
                dve.wait_ge(root_made, k + 1)
                nc.vector.reciprocal(rstd[:, 0:n], std[:, 0:n]).then_inc(rstd_made, 1)
                dve.wait_ge(rstd_made, k + 1)
                wait(dve, stored, 16 * k)
                for t in range(n):
                    last = nc.vector.tensor_scalar(y_out[:, t, :], y[:, t, :], mv[:, t, 0:1], rstd[:, t:t + 1],
                                                   ALU.subtract, ALU.mult)
                last.then_inc(y_normed, 1)

            def step(i):
                for b in range(2):
                    g = 2 * i + b
                    for h in range(2):
                        u = 2 * g + h
                        copy_hotT(u, h)
                        make_hot(g + h, (b + h) % 2, 1 - h, u - 2)
                        if h == 0:
                            if behind(i, 0):
                                add_sums(g - 2, look_up(dve, g - 2, START, n_nodes))
                            keep_window(b, g, product(i, 2 * b), 2 * (g - 1))
                            if b == 1 and behind(i, LAG - 1):
                                take_sums(i - LAG, i - LAG, 2 * i, product(i, 0))
                        else:
                            wait(dve, x_turned, u + 1)
                            nc.vector.tensor_copy(src_now[:, b, :], src_all[:, bass.ds(CH * (g + 2), CH)]
                                                  ).then_inc(src_staged, 1)
                            if b == 0:
                                wait(dve, prod_made, product(i, 1) + 1)
                                nc.vector.tensor_tensor(base[:, bass.ds(i, 1), :], pprod[:, 0:1, :],
                                                        xt[:, :].unsqueeze(1), ALU.add).then_inc(prod_kept, 1)
                                if behind(i, LAG):
                                    normalise(i - LAG - 1)
                            elif behind(i, LAG - 1):
                                keep_tile(i - LAG, i - LAG, product(i, 3))
            make_hot(0, 0, 0, 0)
            dve.wait_ge(src_in, 16)
            dve.wait_ge(ST_cleared, 1)
            windows, late = turns(dve, step)
            add_sums(NG - 2, look_up(dve, NG - 2, START, n_nodes))
            normalise(NI - LAG - 1)
            add_sums(NG - 1, look_up(dve, NG - 1, START, n_nodes))

            def spilled_window(t, g, start):
                u = 2 * (NG + t)
                nc.vector.tensor_copy(src_now[:, 0, :], src_all[:, bass.ds(CH * g, CH)]).then_inc(src_staged, 1)
                d = dloc[:, bass.ds(CH * g, CH)]
                nc.vector.tensor_scalar(d, d, float(-P), None, ALU.add).then_inc(shifted, 1)
                dve.wait_ge(shifted, t + 1)
                make_hot(g, 0, 0, u)
                make_hot(g, 0, 1, u)
                copy_hotT(u, 0)
                keep_window(0, NG + t, PRODUCTS + t, u)
                copy_hotT(u + 1, 1)
                add_sums(NG + t, start)
            spilled(dve, windows, spilled_window)

            take_sums(NT - LAG, NORMS - 1, NG + windows, PRODUCTS + windows, LAG)
            keep_tile(NT - LAG, NORMS - 1, PRODUCTS + windows, LAG)
            normalise(NORMS - 1, LAG)

            def once_more(tile, k, v):
                take_sums(tile, k, NG + windows, v)
                keep_tile(tile, k, v)
                normalise(k)
            redone(dve, windows, late, once_more)


def kernel(x, src, dst, L0_gnn_weight1, L0_gnn_weight2, L0_gnn_loop_weight, L0_gnn_bias):
    import numpy as np
    import concourse.bacc as bacc
    from concourse.bass_utils import run_bass_kernel_spmd as run

    x, src, dst = np.asarray(x), np.asarray(src), np.asarray(dst)
    n_nodes, n_edges = x.shape[0], src.shape[0]
    tiles = -(-n_nodes // P)
    groups = 2 * tiles
    chunks = -(-n_edges // P)
    assert (groups - 1) * CH + HC < chunks <= groups * CH

    def edge_table(a, fill, n):
        a = np.concatenate([a, np.full(n * CH * P - a.shape[0], fill, a.dtype)])
        return np.ascontiguousarray(a.reshape(n * CH, P).T)

    arrays = {
        "x": np.concatenate([x, np.zeros(((tiles + 1) * P - n_nodes, x.shape[1]), x.dtype)]),
        "src": edge_table(src, 0, groups + 2),
        "dst": edge_table(dst, n_nodes, groups),
        "w1": np.asarray(L0_gnn_weight1), "w2": np.asarray(L0_gnn_weight2),
        "wl": np.asarray(L0_gnn_loop_weight), "bias": np.asarray(L0_gnn_bias),
    }
    nc = bacc.Bacc("TRN2", target_bir_lowering=False, num_devices=1)
    aps = [nc.dram_tensor(name, a.shape, mybir.dt.from_np(a.dtype), kind="ExternalInput").ap()
           for name, a in arrays.items()]
    out = nc.dram_tensor("out", (tiles * P, x.shape[1]), F32, kind="ExternalOutput").ap()
    program(nc, *aps, out, n_nodes, chunks)
    r = run(nc, [arrays], core_ids=[0])
    return r.results[0]["out"][:n_nodes]
```
